# Optimizing a Trainium2 kernel written in Bass

```python
import numpy as np
import jax
import jax.numpy as jnp

def _softmax(x, axis=-1):
    return jax.nn.softmax(x, axis=axis)

def _gelu(x):
    return jax.nn.gelu(x, approximate=True)

def _silu(x):
    return jax.nn.silu(x)

def _sigmoid(x):
    return jax.nn.sigmoid(x)

def _layernorm(x, axis=-1, eps=1e-05):
    m = jnp.mean(x, axis=axis, keepdims=True)
    v = jnp.var(x, axis=axis, keepdims=True)
    return (x - m) / jnp.sqrt(v + eps)

def _scatter_add(tgt, idx, src, axis=0):
    return tgt.at[idx].add(src)

def _segment_sum(src, seg, n):
    return jax.ops.segment_sum(src, seg, n)
kernel_name = 'mk_gnn_ffn_d2_gnn_r32_0b074c'

def setup_inputs(seed: int=0):
    np.random.seed(seed)
    _w = jnp.asarray

    def _rec_inputs():
        import jax
        import jax.numpy as jnp
        _gk = jax.random.key(seed)
        x = -8.776e-05 + 1 * jax.random.normal(jax.random.fold_in(_gk, 1), (3125, 256), jnp.float32)
        _s = jax.random.randint(jax.random.fold_in(_gk, 2), (25000,), 0, 3125, jnp.int32)
        _d = jax.random.randint(jax.random.fold_in(_gk, 3), (25000,), 0, 3125, jnp.int32)
        _loop = jnp.arange(3125, dtype=jnp.int32)
        src = jnp.concatenate([_s, _d, _loop])
        dst = jnp.concatenate([_d, _s, _loop])
        _o = jnp.argsort(dst, stable=True)
        src = src[_o]
        dst = dst[_o]
        edge_weight = jax.random.uniform(jax.random.fold_in(_gk, 12), (53125,), jnp.float32, 0.0, 0.999996)
        return (x, src, dst, edge_weight)
    x, src, dst, edge_weight = _rec_inputs()

    def _L0_gnn_setup():
        import jax, jax.numpy as jnp
        import numpy as np
        N_NODES = 625
        N_EDGES = 10000
        D = 256
        NUM_LAYERS = 5

        def gru_cell(m, h, w_ih, w_hh, b_ih, b_hh):
            gi = m @ w_ih.T + b_ih
            gh = h @ w_hh.T + b_hh
            i_r, i_z, i_n = jnp.split(gi, 3, axis=1)
            h_r, h_z, h_n = jnp.split(gh, 3, axis=1)
            r = jax.nn.sigmoid(i_r + h_r)
            z = jax.nn.sigmoid(i_z + h_z)
            n = jnp.tanh(i_n + r * h_n)
            return (1.0 - z) * n + z * h
        key = jax.random.key(seed)
        ks = jax.random.split(key, 8)
        x = jax.random.normal(ks[0], (N_NODES, D), dtype=jnp.float32)
        src = jax.random.randint(ks[1], (N_EDGES,), 0, N_NODES)
        dst = jax.random.randint(ks[2], (N_EDGES,), 0, N_NODES)
        edge_index = jnp.stack([src, dst]).astype(jnp.int64)
        edge_attr = jax.random.uniform(ks[3], (N_EDGES,), dtype=jnp.float32)
        s = 1.0 / np.sqrt(D)
        weight = jax.random.uniform(ks[4], (NUM_LAYERS, D, D), minval=-s, maxval=s, dtype=jnp.float32)
        w_ih = jax.random.uniform(ks[5], (3 * D, D), minval=-s, maxval=s, dtype=jnp.float32)
        w_hh = jax.random.uniform(ks[6], (3 * D, D), minval=-s, maxval=s, dtype=jnp.float32)
        b = jax.random.uniform(ks[7], (2, 3 * D), minval=-s, maxval=s, dtype=jnp.float32)
        return {'x': x, 'edge_index': edge_index, 'edge_attr': edge_attr, 'weight': weight, 'w_ih': w_ih, 'w_hh': w_hh, 'b_ih': b[0], 'b_hh': b[1]}
    _L0_gnn_all = _L0_gnn_setup()
    _L0_gnn_in = {k: v for k, v in _L0_gnn_all.items() if k in ('weight', 'w_ih', 'w_hh', 'b_ih', 'b_hh')}
    del _L0_gnn_all

    def _L0_ffn_setup():
        import jax, jax.numpy as jnp
        import numpy as np
        B, S, D, F, E, K = (8, 64, 256, 1024, 8, 2)
        key = jax.random.key(seed)
        ks = jax.random.split(key, 10)
        s = 0.02
        return {'x': jax.random.normal(ks[0], (B, S, D), dtype=jnp.float32), 'Wr': jax.random.normal(ks[1], (D, E), dtype=jnp.float32) * s, 'W1s': jax.random.normal(ks[2], (D, F), dtype=jnp.float32) * s, 'b1s': jnp.zeros((F,), dtype=jnp.float32), 'W2s': jax.random.normal(ks[3], (F, D), dtype=jnp.float32) * s, 'b2s': jnp.zeros((D,), dtype=jnp.float32), 'W1p': jax.random.normal(ks[4], (E, D, F), dtype=jnp.float32) * s, 'b1p': jnp.zeros((E, F), dtype=jnp.float32), 'W2p': jax.random.normal(ks[5], (E, F, D), dtype=jnp.float32) * s, 'b2p': jnp.zeros((E, D), dtype=jnp.float32)}
    _L0_ffn_all = _L0_ffn_setup()
    _L0_ffn_in = {k: v for k, v in _L0_ffn_all.items() if k in ('Wr', 'W1s', 'b1s', 'W2s', 'b2s', 'W1p', 'b1p', 'W2p', 'b2p')}
    del _L0_ffn_all

    def _L1_gnn_setup():
        import jax, jax.numpy as jnp
        import numpy as np
        NEG_SLOPE = 0.2

        def gatv2_layer(x, Wl, Wr, att, bias, src, dst, n_nodes, heads, ch, concat):
            xl = (x @ Wl).reshape(n_nodes, heads, ch)
            xr = (x @ Wr).reshape(n_nodes, heads, ch)
            m = xl[src] + xr[dst]
            e = jax.nn.leaky_relu(m, NEG_SLOPE)
            logits = jnp.einsum('ehc,hc->eh', e, att)
            mx = jax.ops.segment_max(logits, dst, num_segments=n_nodes)
            ex = jnp.exp(logits - mx[dst])
            denom = jax.ops.segment_sum(ex, dst, num_segments=n_nodes)
            alpha = ex / denom[dst]
            out = jax.ops.segment_sum(alpha[:, :, None] * xl[src], dst, num_segments=n_nodes)
            if concat:
                out = out.reshape(n_nodes, heads * ch)
            else:
                out = out.mean(axis=1)
            return out + bias
        N, E = (50000, 25000)
        IN, HID, OUT, H = (256, 64, 256, 4)
        key = jax.random.key(seed)
        ks = jax.random.split(key, 12)
        s = lambda fan_in: 1.0 / np.sqrt(fan_in)
        return {'x': jax.random.normal(ks[0], (N, IN), dtype=jnp.float32), 'edge_index': jax.random.randint(ks[1], (2, E), 0, N, dtype=jnp.int64), 'Wl1': jax.random.normal(ks[2], (IN, H * HID), jnp.float32) * s(IN), 'Wr1': jax.random.normal(ks[3], (IN, H * HID), jnp.float32) * s(IN), 'att1': jax.random.normal(ks[4], (H, HID), jnp.float32) * s(HID), 'b1': jnp.zeros((H * HID,), jnp.float32), 'Wl2': jax.random.normal(ks[5], (H * HID, OUT), jnp.float32) * s(H * HID), 'Wr2': jax.random.normal(ks[6], (H * HID, OUT), jnp.float32) * s(H * HID), 'att2': jax.random.normal(ks[7], (1, OUT), jnp.float32) * s(OUT), 'b2': jnp.zeros((OUT,), jnp.float32)}
    _L1_gnn_all = _L1_gnn_setup()
    _L1_gnn_in = {k: v for k, v in _L1_gnn_all.items() if k in ('Wl1', 'Wr1', 'att1', 'b1', 'Wl2', 'Wr2', 'att2', 'b2')}
    del _L1_gnn_all

    def _L1_ffn_setup():
        import jax, jax.numpy as jnp
        import numpy as np
        E = 8
        K = 2
        D = 256
        H = 512
        DOUT = 256
        EPS = 1e-05
        key = jax.random.key(seed)
        ks = jax.random.split(key, 9)
        s = 0.02
        return {'x': jax.random.normal(ks[0], (4, 256, D), jnp.float32), 'gamma': 1.0 + 0.05 * jax.random.normal(ks[1], (D,), jnp.float32), 'beta': 0.05 * jax.random.normal(ks[2], (D,), jnp.float32), 'Wr': 0.01 * jax.random.normal(ks[3], (D, E), jnp.float32), 'br': jnp.zeros((E,), jnp.float32), 'W1': s * jax.random.normal(ks[4], (E, D, H), jnp.float32), 'b1': s * jax.random.normal(ks[5], (E, H), jnp.float32), 'W2': s * jax.random.normal(ks[6], (E, H, DOUT), jnp.float32), 'b2': s * jax.random.normal(ks[7], (E, DOUT), jnp.float32)}
    _L1_ffn_all = _L1_ffn_setup()
    _L1_ffn_in = {k: v for k, v in _L1_ffn_all.items() if k in ('gamma', 'beta', 'Wr', 'br', 'W1', 'b1', 'W2', 'b2')}
    del _L1_ffn_all
    return {'x': x, 'src': src, 'dst': dst, 'edge_weight': edge_weight, 'L0_gnn_weight': _L0_gnn_in['weight'], 'L0_gnn_w_ih': _L0_gnn_in['w_ih'], 'L0_gnn_w_hh': _L0_gnn_in['w_hh'], 'L0_gnn_b_ih': _L0_gnn_in['b_ih'], 'L0_gnn_b_hh': _L0_gnn_in['b_hh'], 'L0_ffn_Wr': _L0_ffn_in['Wr'], 'L0_ffn_W1s': _L0_ffn_in['W1s'], 'L0_ffn_b1s': _L0_ffn_in['b1s'], 'L0_ffn_W2s': _L0_ffn_in['W2s'], 'L0_ffn_b2s': _L0_ffn_in['b2s'], 'L0_ffn_W1p': _L0_ffn_in['W1p'], 'L0_ffn_b1p': _L0_ffn_in['b1p'], 'L0_ffn_W2p': _L0_ffn_in['W2p'], 'L0_ffn_b2p': _L0_ffn_in['b2p'], 'L1_gnn_Wl1': _L1_gnn_in['Wl1'], 'L1_gnn_Wr1': _L1_gnn_in['Wr1'], 'L1_gnn_att1': _L1_gnn_in['att1'], 'L1_gnn_b1': _L1_gnn_in['b1'], 'L1_gnn_Wl2': _L1_gnn_in['Wl2'], 'L1_gnn_Wr2': _L1_gnn_in['Wr2'], 'L1_gnn_att2': _L1_gnn_in['att2'], 'L1_gnn_b2': _L1_gnn_in['b2'], 'L1_ffn_gamma': _L1_ffn_in['gamma'], 'L1_ffn_beta': _L1_ffn_in['beta'], 'L1_ffn_Wr': _L1_ffn_in['Wr'], 'L1_ffn_br': _L1_ffn_in['br'], 'L1_ffn_W1': _L1_ffn_in['W1'], 'L1_ffn_b1': _L1_ffn_in['b1'], 'L1_ffn_W2': _L1_ffn_in['W2'], 'L1_ffn_b2': _L1_ffn_in['b2']}

def reference(x, src, dst, edge_weight, L0_gnn_weight, L0_gnn_w_ih, L0_gnn_w_hh, L0_gnn_b_ih, L0_gnn_b_hh, L0_ffn_Wr, L0_ffn_W1s, L0_ffn_b1s, L0_ffn_W2s, L0_ffn_b2s, L0_ffn_W1p, L0_ffn_b1p, L0_ffn_W2p, L0_ffn_b2p, L1_gnn_Wl1, L1_gnn_Wr1, L1_gnn_att1, L1_gnn_b1, L1_gnn_Wl2, L1_gnn_Wr2, L1_gnn_att2, L1_gnn_b2, L1_ffn_gamma, L1_ffn_beta, L1_ffn_Wr, L1_ffn_br, L1_ffn_W1, L1_ffn_b1, L1_ffn_W2, L1_ffn_b2):
    import jax
    import jax.numpy as jnp

    def _L0_gnn_ref(x, edge_index, edge_attr, weight, w_ih, w_hh, b_ih, b_hh):
        import jax, jax.numpy as jnp
        import numpy as np
        N_NODES = 625
        N_EDGES = 10000
        D = 256
        NUM_LAYERS = 5

        def gru_cell(m, h, w_ih, w_hh, b_ih, b_hh):
            gi = m @ w_ih.T + b_ih
            gh = h @ w_hh.T + b_hh
            i_r, i_z, i_n = jnp.split(gi, 3, axis=1)
            h_r, h_z, h_n = jnp.split(gh, 3, axis=1)
            r = jax.nn.sigmoid(i_r + h_r)
            z = jax.nn.sigmoid(i_z + h_z)
            n = jnp.tanh(i_n + r * h_n)
            return (1.0 - z) * n + z * h
        src = edge_index[0]
        dst = edge_index[1]
        n_nodes = x.shape[0]
        h = x
        for i in range(weight.shape[0]):
            m = h @ weight[i]
            msgs = m[src] * edge_attr[:, None]
            agg = jax.ops.segment_sum(msgs, dst, num_segments=n_nodes)
            h = gru_cell(agg, h, w_ih, w_hh, b_ih, b_hh)
        return h

    def _L0_ffn_ref(x, Wr, W1s, b1s, W2s, b2s, W1p, b1p, W2p, b2p):
        import jax, jax.numpy as jnp
        import numpy as np
        B, S, D, F, E, K = (8, 64, 256, 1024, 8, 2)
        gelu = lambda t: jax.nn.gelu(t, approximate=False)
        shared = gelu(x @ W1s + b1s) @ W2s + b2s
        rw = jax.nn.softmax(x @ Wr, axis=-1)
        topw, topi = jax.lax.top_k(rw, K)
        topw = topw / jnp.sum(topw, axis=-1, keepdims=True)
        mask = jnp.sum(jax.nn.one_hot(topi, E, dtype=topw.dtype) * topw[..., None], axis=-2)
        h = gelu(jnp.einsum('bsd,edf->bsef', x, W1p) + b1p)
        priv = jnp.einsum('bsef,efd->bsed', h, W2p) + b2p
        routed = jnp.einsum('bsed,bse->bsd', priv, mask)
        return shared + routed

    def _L1_gnn_ref(x, edge_index, Wl1, Wr1, att1, b1, Wl2, Wr2, att2, b2):
        import jax, jax.numpy as jnp
        import numpy as np
        NEG_SLOPE = 0.2

        def gatv2_layer(x, Wl, Wr, att, bias, src, dst, n_nodes, heads, ch, concat):
            xl = (x @ Wl).reshape(n_nodes, heads, ch)
            xr = (x @ Wr).reshape(n_nodes, heads, ch)
            m = xl[src] + xr[dst]
            e = jax.nn.leaky_relu(m, NEG_SLOPE)
            logits = jnp.einsum('ehc,hc->eh', e, att)
            mx = jax.ops.segment_max(logits, dst, num_segments=n_nodes)
            ex = jnp.exp(logits - mx[dst])
            denom = jax.ops.segment_sum(ex, dst, num_segments=n_nodes)
            alpha = ex / denom[dst]
            out = jax.ops.segment_sum(alpha[:, :, None] * xl[src], dst, num_segments=n_nodes)
            if concat:
                out = out.reshape(n_nodes, heads * ch)
            else:
                out = out.mean(axis=1)
            return out + bias
        N = x.shape[0]
        loops = jnp.arange(N, dtype=edge_index.dtype)
        src = jnp.concatenate([edge_index[0], loops])
        dst = jnp.concatenate([edge_index[1], loops])
        h = gatv2_layer(x, Wl1, Wr1, att1, b1, src, dst, N, 4, 64, concat=True)
        h = jax.nn.elu(h)
        out = gatv2_layer(h, Wl2, Wr2, att2, b2, src, dst, N, 1, 256, concat=False)
        return out

    def _L1_ffn_ref(x, gamma, beta, Wr, br, W1, b1, W2, b2):
        import jax, jax.numpy as jnp
        import numpy as np
        E = 8
        K = 2
        D = 256
        H = 512
        DOUT = 256
        EPS = 1e-05
        mu = jnp.mean(x, axis=-1, keepdims=True)
        var = jnp.mean(jnp.square(x - mu), axis=-1, keepdims=True)
        xn = (x - mu) * jax.lax.rsqrt(var + EPS) * gamma + beta
        logits = jnp.einsum('bsd,de->bse', xn, Wr) + br
        top_vals, top_idx = jax.lax.top_k(logits, K)
        w = jax.nn.softmax(top_vals, axis=-1)
        w_full = jnp.einsum('bsk,bske->bse', w, jax.nn.one_hot(top_idx, E, dtype=w.dtype))
        y = jnp.zeros(x.shape[:-1] + (DOUT,), x.dtype)
        for e in range(E):
            h = jax.nn.gelu(jnp.einsum('bsd,dh->bsh', xn, W1[e]) + b1[e], approximate=False)
            y_e = jnp.einsum('bsh,hd->bsd', h, W2[e]) + b2[e]
            y = y + y_e * w_full[..., e, None]
        return y
    edge_index = jnp.stack([src, dst])
    x = x + _L0_gnn_ref(_layernorm(x, axis=-1), edge_index, edge_weight, L0_gnn_weight, L0_gnn_w_ih, L0_gnn_w_hh, L0_gnn_b_ih, L0_gnn_b_hh)
    x = x + _L0_ffn_ref(_layernorm(x, axis=-1)[None], L0_ffn_Wr, L0_ffn_W1s, L0_ffn_b1s, L0_ffn_W2s, L0_ffn_b2s, L0_ffn_W1p, L0_ffn_b1p, L0_ffn_W2p, L0_ffn_b2p)[0]
    x = x + _L1_gnn_ref(_layernorm(x, axis=-1), edge_index, L1_gnn_Wl1, L1_gnn_Wr1, L1_gnn_att1, L1_gnn_b1, L1_gnn_Wl2, L1_gnn_Wr2, L1_gnn_att2, L1_gnn_b2)
    x = x + _L1_ffn_ref(_layernorm(x, axis=-1)[None], L1_ffn_gamma, L1_ffn_beta, L1_ffn_Wr, L1_ffn_br, L1_ffn_W1, L1_ffn_b1, L1_ffn_W2, L1_ffn_b2)[0]
    return x

_drawn_inputs = setup_inputs


def setup_inputs(seed=0):
    import zlib

    import numpy as np

    out = dict(_drawn_inputs(seed))
    spreads = {'L0_ffn_b1s': (0.0, 0.1),
     'L0_ffn_b2s': (0.0, 0.1),
     'L0_ffn_b1p': (0.0, 0.315),
     'L0_ffn_b2p': (0.0, 0.1),
     'L1_gnn_b1': (0.0, 0.1),
     'L1_gnn_b2': (0.0, 0.1),
     'L1_ffn_br': (0.0, 0.1)}
    factors = {'L1_gnn_Wr1': 3.392,
     'L1_gnn_Wr2': 8.0,
     'L1_gnn_att2': 4.871,
     'L1_ffn_gamma': 5.402,
     'L1_ffn_beta': 5.06,
     'L1_ffn_b1': 8.0,
     'L1_ffn_b2': 4.41}
    for name, (base, spread) in spreads.items():
        noise = np.random.default_rng([zlib.crc32(name.encode()), seed]).standard_normal(out[name].shape)
        drawn = base * np.exp(spread * noise) if base else spread * noise
        out[name] = jnp.asarray(drawn.astype(out[name].dtype))
    for name, factor in factors.items():
        out[name] = (out[name] * factor).astype(out[name].dtype)
    return out
```

```python
import numpy as np
from contextlib import ExitStack
import concourse.bass as bass
from concourse import mybir

F32 = mybir.dt.float32
I32 = mybir.dt.int32
ALU = mybir.AluOpType
ACT = mybir.ActivationFunctionType
AX = mybir.AxisListType

P = 128
NODES = 3125
D = 256
EDGES = 53125
NT = -(-NODES // P)
NPAD = NT * P
FULL_ROWS = EDGES // P
TAIL = EDGES - FULL_ROWS * P
EROWS = FULL_ROWS + 1
PAIRS = EROWS + NT - 1
HALF = 4
UNR = 2 * HALF
TURNS = PAIRS // UNR
GROUPS = 4
RPG = PAIRS // GROUPS
assert TURNS * UNR == PAIRS and GROUPS * RPG == PAIRS
LAYERS = 5
HEADS = 4
AHEAD = 8
GD = 3 * D
SUBS = ((0, 384), (384, 256))
CH = 5
NCH = NT // CH
CHN = CH * P
PAD_DST = 100000
NEG = -1.0e30
SPLIT = 125
OWN = EDGES // SPLIT


def program(nc, a, out):
    ctx = ExitStack()
    with ctx:
        def sb(name, shape, dt=F32):
            return ctx.enter_context(nc.sbuf_tensor(name, shape, dt))

        sems = {}

        def sem(name):
            if name not in sems:
                sems[name] = ctx.enter_context(nc.semaphore(name))
            return sems[name]

        ctx.enter_context(nc.allow_non_contiguous_dma(reason="bias columns and edge-row padding"))
        PS = ctx.enter_context(nc.psum_tensor("PS", [P, 8, 512], F32))
        X = sb("X", [P, NT, D])
        ident = sb("ident", [P, P])
        iota_row = sb("iota_row", [P, P])
        SRC = sb("SRC", [P, PAIRS], I32)
        DR = sb("DR", [P, PAIRS + AHEAD])
        WE = sb("WE", [P, PAIRS + AHEAD])
        EN = sb("EN", [P, PAIRS])
        brow = sb("brow", [1, PAIRS], I32)
        F_ROW = sb("F_ROW", [RPG, GROUPS, P])
        E_ROW = sb("E_ROW", [RPG, GROUPS, P])
        V_ROW = sb("V_ROW", [RPG, GROUPS, P])
        LEAD = sb("LEAD", [RPG, GROUPS, P])
        TRAIL = sb("TRAIL", [RPG, GROUPS, P])
        row_start = sb("row_start", [HEADS, PAIRS])
        row_end = sb("row_end", [HEADS, PAIRS])
        arena = sb("arena", [P, 39464])
        small = sb("small", [P, 512])

        def cut(buf, at, shape, parts=P):
            n = int(np.prod(shape))
            v = buf[0:parts, at:at + n]
            if len(shape) == 2:
                v = v.rearrange("p (a b) -> p a b", a=shape[0])
            if len(shape) == 3:
                v = v.rearrange("p (a b c) -> p a b c", a=shape[0], b=shape[1])
            return v

        rows_i = nc.dram_tensor("rows_i", [EROWS, 4 * P], I32).ap()
        rows_w = nc.dram_tensor("rows_w", [EROWS, P], F32).ap()
        table = nc.dram_tensor("table", [NPAD, D], F32).ap()
        rv = rows_i.rearrange("t (s e) -> t s e", s=4)

        ones = arena[:, 12000:12000 + P]
        iota_i = arena[:, 12200:12200 + P].bitcast(I32)
        dst_i = arena[0:SPLIT, 0:OWN].bitcast(I32)
        dst_f = arena[0:SPLIT, 512:512 + OWN]
        cnt_junk = arena[0:SPLIT, 1024:1024 + OWN]
        rowi_buf = cut(arena, 2048, (GROUPS, 4 * P), RPG)
        rowi = rowi_buf.bitcast(I32)
        roww = cut(arena, 4096, (GROUPS, P), RPG)
        rowf = cut(arena, 4608, (GROUPS, 4 * P), RPG)
        dr_row = cut(arena, 6656, (GROUPS, P), RPG)
        t0_row = cut(arena, 7168, (GROUPS, P), RPG)
        padi = arena[0:1, 7680:7680 + 1024].bitcast(I32)
        padf = arena[0:1, 8704:8704 + 256]
        jrow = arena[:, 9000:9000 + PAIRS]
        jrow_i = arena[:, 9500:9500 + PAIRS].bitcast(I32)
        bacc = [arena[:, 10000 + 512 * i:10000 + 512 * i + PAIRS] for i in range(2)]
        cnt = small[:, 0:24]
        tot_i = small[:, 32:56].bitcast(I32)
        thr = small[:, 64:88]
        jcol = small[0:RPG, 96:100]
        jcol_i = small[0:RPG, 100:104].bitcast(I32)
        cmp = small[0:RPG, 128:128 + 4 * 24].rearrange("p (g b) -> p g b", g=4)
        bcol = small[0:RPG, 256:260]
        tcol = small[0:RPG, 260:264]
        tcol_i = small[0:RPG, 264:268].bitcast(I32)
        blo = small[0:RPG, 272:276]
        NB = NT - 1
        any_start = small[0:RPG, 288:304].rearrange("p (g h) -> p g h", g=GROUPS)
        any_end = small[0:RPG, 304:320].rearrange("p (g h) -> p g h", g=GROUPS)

        HT = cut(arena, 0, (2, NPAD))
        AG = cut(arena, 6400, (2, NPAD))
        HN = cut(arena, 12800, (NT, D))
        G = cut(arena, 19200, (UNR, D))
        PM = cut(arena, 21248, (UNR, P))
        WI = cut(arena, 22272, (2, GD))
        WHT = cut(arena, 23808, (2, GD))
        WIT = cut(arena, 25344, (2, GD))
        WL = cut(arena, 26880, (2, D))
        WLT = cut(arena, 27392, (2, D))
        rawT = HT
        b_raw = small[:, 0:12]
        b_rz = small[:, 16:20]
        gbuf = cut(arena, 28000, (8, 384)).rearrange("p (a f) n -> p a f n", a=4)
        idx = sb("idx", [P, 2, HALF], I32)
        mv = sb("mv", [P, NT, 2])
        st = sb("st", [P, NT, 6])
        rstd = sb("rstd", [P, NT])
        std = sb("std", [P, NT])
        eps = sb("eps", [P, 1])

        FFN0 = dict(tag="f0", E=8, Fh=1024, shared=True, Wr=a["L0_ffn_Wr"], W1=a["L0_ffn_W1p"], b1=a["L0_ffn_b1p"],
                    W2=a["L0_ffn_W2p"], b2=a["L0_ffn_b2p"], W1s=a["L0_ffn_W1s"], b1s=a["L0_ffn_b1s"], W2s=a["L0_ffn_W2s"],
                    b2s=a["L0_ffn_b2s"])
        FFN1 = dict(tag="f1", E=8, Fh=512, shared=False, Wr=a["L1_ffn_Wr"], W1=a["L1_ffn_W1"], b1=a["L1_ffn_b1"],
                    W2=a["L1_ffn_W2"], b2=a["L1_ffn_b2"], br=a["L1_ffn_br"], gamma=a["L1_ffn_gamma"], beta=a["L1_ffn_beta"])
        YT = cut(arena, 0, (2, NPAD))
        YN = cut(arena, 6400, (NT, D))
        W1B = [cut(arena, 12800 + 2048 * i, (2, 1024)) for i in range(2)]
        W2B = [cut(arena, 16896 + 2048 * i, (8, D)) for i in range(2)]
        HID = [cut(arena, 20992 + 3072 * i, (8, 384)) for i in range(2)]
        B1B = [arena[:, 27136 + 8 * i:27144 + 8 * i] for i in range(2)]
        WRB = cut(arena, 27200, (2, 8))
        BRB = arena[:, 27216:27224]
        GBT = arena[:, 27224:27228]
        B2B = arena[0:9, 27264:27264 + D]
        MSK = cut(arena, 27520, (NT, 9))
        MSKT = arena[0:9, 27776:27776 + NPAD]
        LG = [cut(arena, 31000 + 256 * i, (NT, 8)) for i in range(6)]
        TOP = [arena[:, 32600 + 32 * i:32600 + 32 * i + NT] for i in range(8)]
        io8 = iota_row[:, 0:8].unsqueeze(1).to_broadcast([P, NT, 8])

        GAT1 = dict(tag="g1", H=4, no=0, Wl=a["L1_gnn_Wl1"], Wr=a["L1_gnn_Wr1"], att=a["L1_gnn_att1"], b=a["L1_gnn_b1"], last=False)
        GAT2 = dict(tag="g2", H=1, no=1, Wl=a["L1_gnn_Wl2"], Wr=a["L1_gnn_Wr2"], att=a["L1_gnn_att2"], b=a["L1_gnn_b2"], last=True)
        PER_LAYER = dict(_free=1, _w=64, _table=16 * NCH, _lin=NCH, _xmm=NT, _xlr=NT, _node=1, a_sel=PAIRS + AHEAD,
                         a_tp=PAIRS + HALF, a_pt=PAIRS + HALF, a_pair=PAIRS + UNR, a_lg=PAIRS + HALF, a_lk=2 * PAIRS,
                         _logits=1, _rows=GROUPS, _scans=1, _ends=1, _carry=1, _back=1, _shift=1, _ex=1, _cols=1, _exm=1,
                         b_gx=PAIRS, b_sel=PAIRS + HALF, b_pair=PAIRS + UNR, b_acc=PAIRS + HALF, _sh2=1, _e2=2,
                         _neg=NCH, _eneg=NCH, _yn=1)

        def since(g, name):
            return g["no"] * PER_LAYER[name]

        TW = D + HEADS
        table2 = nc.dram_tensor("table2", [NPAD, TW], F32).ap()
        tb2 = table2.rearrange("(t p) f -> p t f", p=P)
        XLR = cut(arena, 0, (NT, 2, TW))
        ACC = cut(arena, 13000, (NT, 265))
        YTG = cut(arena, 13000, (2, NPAD))
        G2 = cut(arena, 19632, (UNR, TW))
        PM2 = cut(arena, 21712, (UNR, P))
        PT2 = cut(arena, 22736, (UNR, P))
        EXM = cut(arena, 23760, (PAIRS, 9))
        LGT = cut(arena, 27720, (PAIRS, HEADS))
        ROWA = cut(arena, 29480, (GROUPS, HEADS, P), RPG)
        ROWB = cut(arena, 31528, (GROUPS, HEADS, P), RPG)
        ROWC = cut(arena, 33576, (GROUPS, HEADS, P), RPG)
        GX = cut(arena, 35624, (UNR, D))
        YNG = cut(arena, 29480, (NT, D))
        TMP = cut(arena, 35880, (CH, D))
        WLR = cut(arena, 37672, (2, 512))
        ATT8 = arena[:, 38696:38952]
        ATT2 = arena[:, 38952:39208]
        BIAS = arena[:, 39208:39464]
        TMPP = cut(arena, 21712, (2, D))
        SELF = sb("SELF", [P, NT, HEADS])
        NODE = [sb(f"NODE{i}", [P, NT, HEADS]) for i in range(4)]
        REL = sb("REL", [P, UNR, HEADS])
        ROWH = [arena[0:HEADS, 36000 + 500 * i:36000 + 500 * i + PAIRS + 1] for i in range(2)]
        COLH = cut(arena, 37000, (2, GROUPS, HEADS), RPG)

        block = ctx.enter_context(nc.Block())

        tb = table.rearrange("(t p) f -> p t f", p=P)

        @block.sync
        def _(sp):
            def ffn_sp(f):
                t, Fh, E = f["tag"], f["Fh"], f["E"]
                MF = Fh // P
                sp.wait_ge(sem(t + "_free"), 1)
                sp.dma_start(WRB, f["Wr"].rearrange("(c p) e -> p c e", p=P)).then_inc(sem(t + "_small"), 16)
                sp.dma_start(B2B[0:E, :], f["b2"]).then_inc(sem(t + "_small"), 16)
                if f["shared"]:
                    sp.dma_start(B2B[E:E + 1, :], f["b2s"].rearrange("(o n) -> o n", o=1)).then_inc(sem(t + "_small"), 16)
                else:
                    sp.dma_start(BRB, f["br"].rearrange("(o n) -> o n", o=1).to_broadcast([P, E])).then_inc(sem(t + "_small"), 16)
                    sp.dma_start(GBT[:, 0:2], f["gamma"].rearrange("(c p) -> p c", p=P)).then_inc(sem(t + "_small"), 16)
                    sp.dma_start(GBT[:, 2:4], f["beta"].rearrange("(c p) -> p c", p=P)).then_inc(sem(t + "_small"), 16)

                def load(w, w1, b1, w2):
                    sp.dma_start(W1B[w][:, :, 0:Fh], w1.rearrange("(c p) n -> p c n", p=P)).then_inc(sem(f"{t}_w{w}"), 16)
                    sp.dma_start(B1B[w][:, 0:MF], b1.rearrange("(m p) -> p m", p=P)).then_inc(sem(f"{t}_w{w}"), 16)
                    sp.dma_start(W2B[w][:, 0:MF, :], w2.rearrange("(m p) n -> p m n", p=P)).then_inc(sem(f"{t}_w{w}"), 16)

                first = 0
                if f["shared"]:
                    load(1, f["W1s"], f["b1s"], f["W2s"])
                    first = 1
                with sp.Fori(0, E // 2) as e:
                    for w in range(2):
                        sp.wait_ge(sem(t + "_y"), (e * 2 + (w + first + 1)) * NT)
                        one = lambda x: x[bass.ds(e * 2 + w, 1)]
                        load(w, one(f["W1"]).rearrange("o k n -> (o k) n"), one(f["b1"]).rearrange("o n -> (o n)"),
                             one(f["W2"]).rearrange("o k n -> (o k) n"))

            def gat_sp(g):
                t = g["tag"]
                sp.wait_ge(sem("g_free"), 1 + since(g, "_free"))
                sp.dma_start(WLR[:, :, 0:D], g["Wl"].rearrange("(c p) n -> p c n", p=P)).then_inc(sem("g_w"), 16)
                sp.dma_start(WLR[:, :, D:2 * D], g["Wr"].rearrange("(c p) n -> p c n", p=P)).then_inc(sem("g_w"), 16)
                sp.dma_start(ATT8, g["att"].rearrange("h c -> (h c)").rearrange("(o n) -> o n", o=1).to_broadcast([P, D])).then_inc(sem("g_w"), 16)
                sp.dma_start(BIAS, g["b"].rearrange("(o n) -> o n", o=1).to_broadcast([P, D])).then_inc(sem("g_w"), 16)
                for c in range(NCH):
                    sp.wait_ge(sem("g_lin"), c + 1 + since(g, "_lin"))
                    sp.dma_start(tb2[:, c * CH:(c + 1) * CH, :], XLR[:, c * CH:(c + 1) * CH, 0, :]).then_inc(sem("g_table"), 16)
            sp.dma_start(X[:, 0:NT - 1, :], a["x"][0:(NT - 1) * P, :].rearrange("(t p) f -> p t f", p=P)).then_inc(sem("x_in"), 16)
            sp.wait_ge(sem("x_zero"), 1)
            sp.dma_start(X[0:NODES - (NT - 1) * P, NT - 1, :], a["x"][(NT - 1) * P:NODES, :]).then_inc(sem("x_in"), 16)
            sp.dma_start(dst_i, a["dst"].rearrange("(p n) -> p n", p=SPLIT)).then_inc(sem("dst_in"), 16)
            last = FULL_ROWS
            m = sem("rows_in")
            src, dst, ew = a["src"], a["dst"], a["edge_weight"]

            def rows(n, at):
                return at[0:n * P].rearrange("(t e) -> t e", e=P)
            sp.dma_start(rv[1:last, 0, :], rows(last - 1, dst[P - 1:])).then_inc(m, 16)
            sp.dma_start(rv[0:1, 0, 1:P], dst[0:P - 1].rearrange("(o e) -> o e", o=1)).then_inc(m, 16)
            sp.dma_start(rv[last:, 0, 0:TAIL], dst[last * P - 1:EDGES - 1].rearrange("(o e) -> o e", o=1)).then_inc(m, 16)
            sp.dma_start(rv[0:last, 1, :], rows(last, dst)).then_inc(m, 16)
            sp.dma_start(rv[last:, 1, 0:TAIL], dst[last * P:].rearrange("(o e) -> o e", o=1)).then_inc(m, 16)
            sp.dma_start(rv[0:last, 2, :], rows(last, dst[1:])).then_inc(m, 16)
            sp.dma_start(rv[last:, 2, 0:TAIL - 1], dst[last * P + 1:].rearrange("(o e) -> o e", o=1)).then_inc(m, 16)
            sp.dma_start(rv[0:last, 3, :], rows(last, src)).then_inc(m, 16)
            sp.dma_start(rv[last:, 3, 0:TAIL], src[last * P:].rearrange("(o e) -> o e", o=1)).then_inc(m, 16)
            sp.dma_start(rows_w[0:last, :], rows(last, ew)).then_inc(m, 16)
            sp.dma_start(rows_w[last:, 0:TAIL], ew[last * P:].rearrange("(o e) -> o e", o=1)).then_inc(m, 16)
            sp.wait_ge(sem("pads"), 5)
            sp.dma_start(rv[0:1, 0, 0:1], padi[0:1, 600:601]).then_inc(m, 16)
            sp.dma_start(rv[last:, 0, TAIL:], padi[0:1, 0:P - TAIL]).then_inc(m, 16)
            sp.dma_start(rv[last:, 1, TAIL:], padi[0:1, 0:P - TAIL]).then_inc(m, 16)
            sp.dma_start(rv[last:, 2, TAIL - 1:], padi[0:1, 0:P - TAIL + 1]).then_inc(m, 16)
            sp.dma_start(rv[last:, 3, TAIL:], padi[0:1, 256:256 + P - TAIL]).then_inc(m, 16)
            sp.dma_start(rows_w[last:, TAIL:], padf[0:1, 0:P - TAIL]).then_inc(m, 16)
            sp.wait_ge(sem("meta_end"), 1)
            sp.dma_start(cut(arena, 0, (6, D)), a["L0_gnn_w_ih"].rearrange("(m p) k -> p m k", p=P)).then_inc(sem("wg_in"), 16)
            sp.dma_start(cut(arena, 1536, (6, D)), a["L0_gnn_w_hh"].rearrange("(m p) k -> p m k", p=P)).then_inc(sem("wg_in"), 16)
            sp.dma_start(b_raw[:, 0:6], a["L0_gnn_b_ih"].rearrange("(m p) -> p m", p=P)).then_inc(sem("wg_in"), 16)
            sp.dma_start(b_raw[:, 6:12], a["L0_gnn_b_hh"].rearrange("(m p) -> p m", p=P)).then_inc(sem("wg_in"), 16)
            sp.wait_ge(sem("ln0_y"), NT)
            for c in range(NCH):
                sp.dma_start(tb[:, c * CH:(c + 1) * CH, :], HN[:, c * CH:(c + 1) * CH, :]).then_inc(sem("table_in"), 16)
            with sp.Fori(0, LAYERS) as l:
                sp.wait_ge(sem("fold_free"), l + 1)
                sp.dma_start(WL, a["L0_gnn_weight"][bass.ds(l, 1), :, :].rearrange("o (c p) f -> p (o c) f", p=P)).then_inc(sem("wl_in"), 16)
                for c in range(NCH):
                    sp.wait_ge(sem("tp_free"), l * NT + (CH + (c + 1) * CH))
                    sp.dma_start(tb[:, c * CH:(c + 1) * CH, :], HN[:, c * CH:(c + 1) * CH, :]).then_inc(sem("table_in"), 16)
            sp.wait_ge(sem("x1"), 1)
            ffn_sp(FFN0)
            gat_sp(GAT1)
            gat_sp(GAT2)
            ffn_sp(FFN1)
            sp.wait_ge(sem("x4"), 1)
            sp.dma_start(out.rearrange("(o n) f -> o n f", o=1)[0, 0:(NT - 1) * P, :].rearrange("(t p) f -> p t f", p=P), X[:, 0:NT - 1, :]).then_inc(sem("out"), 16)
            sp.dma_start(out[(NT - 1) * P:NODES, :], X[0:NODES - (NT - 1) * P, NT - 1, :]).then_inc(sem("out"), 16)
            sp.wait_ge(sem("out"), 32)
            sp.wait_ge(sem("table_in"), 16 * NCH * (LAYERS + 1))

        @block.gpsimd
        def _(pool):
            def gather_pairs(no, used, before):
                with pool.Fori(0, TURNS) as k:
                    for h in range(2):
                        pool.wait_ge(sem(used), k * UNR + (h * HALF + HALF + before))
                        pool.tensor_copy(idx[:, h, :], SRC[:, bass.ds(k * UNR + h * HALF, HALF)]).then_inc(sem("idx_in"), 1)
                        pool.wait_ge(sem("idx_in"), k * 2 + ((LAYERS + no) * 2 * TURNS + h + 1))
                        pool.sem_inc(sem("pool_passed"), 1)
                        for i in range(HALF):
                            s = h * HALF + i
                            pool.indirect_dma_start(out=G2[:, s, :], out_offset=None, in_=table2,
                                                    in_offset=bass.IndirectOffsetOnAxis(ap=idx[:, h, i:i + 1], axis=0)
                                                    ).then_inc(sem(f"gath{s}"), 16)

            def gat_pool(g):
                t = g["tag"]
                pool.sem_inc(sem("ga_pair"), UNR)
                pool.wait_ge(sem("g_table"), 16 * NCH + since(g, "_table"))
                gather_pairs(2 * g["no"], "ga_pair", since(g, "a_pair"))
                pool.sem_inc(sem("gb_pair"), UNR)
                pool.wait_ge(sem("ga_pair"), PAIRS + UNR + since(g, "a_pair"))
                gather_pairs(2 * g["no"] + 1, "gb_pair", since(g, "b_pair"))
            pool.memset(X[:, NT - 1, :], 0.0).then_inc(sem("x_zero"), 1)
            pool.memset(ident[:, :], 0.0).then_inc(sem("id"), 1)
            pool.memset(ones, 1.0).then_inc(sem("ones"), 1)
            pool.wait_ge(sem("id"), 1)
            pool.affine_select(out=ident[:, :], in_=ident[:, :], compare_op=ALU.not_equal, fill=1.0,
                               base=0, pattern=[[-1, P]], channel_multiplier=1).then_inc(sem("id"), 1)
            pool.iota(iota_i, pattern=[[1, P]], base=0, channel_multiplier=0).then_inc(sem("iotas"), 1)
            pool.iota(jrow_i, pattern=[[1, PAIRS]], base=0, channel_multiplier=0).then_inc(sem("iotas"), 1)
            pool.iota(jcol_i, pattern=[[RPG, GROUPS]], base=0, channel_multiplier=1).then_inc(sem("iotas"), 1)
            pool.iota(padi[0:1, 0:256], pattern=[[0, 256]], base=PAD_DST, channel_multiplier=0).then_inc(sem("pads"), 1)
            pool.iota(padi[0:1, 256:512], pattern=[[0, 256]], base=0, channel_multiplier=0).then_inc(sem("pads"), 1)
            pool.iota(padi[0:1, 600:601], pattern=[[0, 1]], base=-1, channel_multiplier=0).then_inc(sem("pads"), 1)
            pool.memset(padf[0:1, :], 0.0).then_inc(sem("pads"), 2)
            pool.wait_ge(sem("rows_in"), 16 * 17)
            pool.wait_ge(sem("tcol"), 1)
            for g in range(GROUPS):
                off = bass.IndirectOffsetOnAxis(ap=tcol_i[:, g:g + 1], axis=0)
                pool.indirect_dma_start(out=rowi[:, g, :], out_offset=None, in_=rows_i, in_offset=off).then_inc(sem("rowmeta"), 16)
                pool.indirect_dma_start(out=roww[:, g, :], out_offset=None, in_=rows_w, in_offset=off).then_inc(sem("rowmeta"), 16)
            pool.sem_inc(sem("pair_used"), UNR)
            with pool.Fori(0, LAYERS) as l:
                pool.wait_ge(sem("table_in"), l * (16 * NCH) + 16 * NCH)
                pool.sem_inc(sem("pool_passed"), 1)
                with pool.Fori(0, TURNS) as k:
                    for h in range(2):
                        base = l * PAIRS + k * UNR
                        pool.wait_ge(sem("pair_used"), base + (h * HALF + HALF))
                        pool.tensor_copy(idx[:, h, :], SRC[:, bass.ds(k * UNR + h * HALF, HALF)]).then_inc(sem("idx_in"), 1)
                        pool.wait_ge(sem("idx_in"), l * (2 * TURNS) + (k * 2 + (h + 1)))
                        pool.sem_inc(sem("pool_passed"), 1)
                        for i in range(HALF):
                            s = h * HALF + i
                            pool.indirect_dma_start(out=G[:, s, :], out_offset=None, in_=table,
                                                    in_offset=bass.IndirectOffsetOnAxis(ap=idx[:, h, i:i + 1], axis=0)
                                                    ).then_inc(sem(f"gath{s}"), 16)
            gat_pool(GAT1)
            gat_pool(GAT2)

        @block.vector
        def _(v):
            chain = [0]

            def link(ins):
                chain[0] += 1
                ins.then_inc(sem("dve_chain"), 1)

            def join():
                v.wait_ge(sem("dve_chain"), chain[0])

            def norm(tag, dst):
                stats(tag, X, dst)

            def stats(tag, src, dst):
                for t in range(NT):
                    link(v.bn_stats(st[:, t, :], src[:, t, :]))
                join()
                for t in range(NT):
                    link(v.bn_aggr(mv[:, t, :], st[:, t, :]))
                join()
                v.sem_inc(sem(tag + "_mv"), 1)
                v.wait_ge(sem(tag + "_std"), 1)
                link(v.reciprocal(rstd[:, :], std[:, :]))
                join()
                for t in range(NT):
                    link(v.tensor_scalar(dst[:, t, :], src[:, t, :], mv[:, t, 0:1], rstd[:, t:t + 1], ALU.subtract, ALU.mult))
                join()

            def ffn_dve(f):
                t, Fh, E = f["tag"], f["Fh"], f["E"]
                EC = E + (1 if f["shared"] else 0)
                v.sem_inc(sem(t + "_free"), 1)
                norm(t + "n", YN)
                if not f["shared"]:
                    stats(t + "m", YN, YN)
                v.sem_inc(sem(t + "_yn"), 1)
                v.wait_ge(sem(t + "_small"), 48 if f["shared"] else 80)
                v.wait_ge(sem(t + "_gate"), 1)
                lg, eq, cand, oh1, oh2, tmp = LG
                m1, mn, m2, d, w1, w2, ed, _ = TOP
                wide = lambda x: x.unsqueeze(2).to_broadcast([P, NT, E])
                gate = PS[:, 7, 0:NT * E].rearrange("p (t e) -> p t e", t=NT)
                if f["shared"]:
                    link(v.tensor_copy(lg, gate))
                else:
                    link(v.tensor_tensor(lg, gate, BRB.unsqueeze(1).to_broadcast([P, NT, E]), ALU.add))
                join()
                for top, hot in ((m1, oh1), (m2, oh2)):
                    link(v.tensor_reduce(top, lg, AX.X, ALU.max))
                    join()
                    link(v.tensor_tensor(eq, lg, wide(top), ALU.is_equal))
                    join()
                    link(v.tensor_scalar(eq, eq, -99.0, 99.0, ALU.mult, ALU.add))
                    join()
                    link(v.tensor_tensor(cand, eq, io8, ALU.add))
                    join()
                    link(v.tensor_reduce(mn, cand, AX.X, ALU.min))
                    join()
                    link(v.tensor_tensor(hot, io8, wide(mn), ALU.is_equal))
                    join()
                    link(v.tensor_scalar(tmp, hot, NEG, None, ALU.mult))
                    join()
                    link(v.tensor_tensor(lg, lg, tmp, ALU.add))
                    join()
                link(v.tensor_tensor(d, m2, m1, ALU.subtract))
                join()
                v.sem_inc(sem(t + "_d"), 1)
                v.wait_ge(sem(t + "_ed"), 1)
                link(v.tensor_scalar(w2, ed, 1.0, None, ALU.add))
                join()
                link(v.reciprocal(w1, w2))
                join()
                link(v.tensor_tensor(w2, w1, ed, ALU.mult))
                join()
                link(v.tensor_tensor(oh1, oh1, wide(w1), ALU.mult))
                link(v.tensor_tensor(oh2, oh2, wide(w2), ALU.mult))
                link(v.memset(MSK, 1.0))
                join()
                link(v.tensor_tensor(MSK[:, :, 0:E], oh1, oh2, ALU.add))
                join()
                v.sem_inc(sem(t + "_msk"), 1)
                v.sem_inc(sem(t + "_yfree"), CH)
                for i in range(NT):
                    v.wait_ge(sem(t + "_b2"), i + 1)
                    v.tensor_tensor(X[:, i, :], X[:, i, :], PS[:, 3 + i % CH, 0:D], ALU.add).then_inc(sem(t + "_b2free"), 1)
                v.wait_ge(sem(t + "_b2free"), NT)

                def add(e, column):
                    with v.Fori(0, NCH) as c:
                        for i in range(CH):
                            q = e * NT + (c * CH + i)
                            v.wait_ge(sem(t + "_y"), q + (2 * NT + 1))
                            v.wait_ge(sem(t + "_yfree"), q + (CH - 1))
                            at = X[:, bass.ds(c * CH + i, 1), :].rearrange("p o n -> p (o n)")
                            w = MSK[:, bass.ds(c * CH + i, 1), :].rearrange("p o e -> p (o e)")
                            v.scalar_tensor_tensor(out=at, in0=PS[:, 3 + i, 0:D], scalar=w[:, bass.ds(column, 1)], in1=at,
                                                   op0=ALU.mult, op1=ALU.add).then_inc(sem(t + "_yfree"), 1)
                first = 0
                if f["shared"]:
                    add(0, E)
                    first = 1
                with v.Fori(0, E // 2) as e:
                    for w in range(2):
                        add(e * 2 + (w + first), e * 2 + w)
                v.wait_ge(sem(t + "_yfree"), CH + EC * NT)

            def gat_dve(g):
                t, H = g["tag"], g["H"]
                C = D // H
                W = 2 * H + 1
                v.sem_inc(sem("g_free"), 1)
                if not g["last"]:
                    norm(t + "n", YNG)
                v.sem_inc(sem("g_yn"), 1)
                v.wait_ge(sem("g_w"), 64 + since(g, "_w"))
                link(v.tensor_scalar(ATT2, ATT8, 0.2, None, ALU.mult))
                join()
                link(v.tensor_scalar(ATT8, ATT8, 0.8, None, ALU.mult))
                join()
                hc = lambda x: x.rearrange("p a (h c) -> p a h c", h=H)
                for c in range(NCH):
                    T = slice(c * CH, (c + 1) * CH)
                    v.wait_ge(sem("g_xlr"), (c + 1) * CH + since(g, "_xlr"))
                    for side in range(2):
                        link(v.tensor_tensor(TMP, XLR[:, T, side, 0:D], ATT2.unsqueeze(1).to_broadcast([P, CH, D]), ALU.mult))
                        join()
                        link(v.tensor_reduce(XLR[:, T, side, D:D + H], hc(TMP), AX.X, ALU.add))
                        join()
                    v.sem_inc(sem("g_lin"), 1)
                    link(v.tensor_tensor(TMP, XLR[:, T, 0, 0:D], XLR[:, T, 1, 0:D], ALU.add))
                    join()
                    link(v.scalar_tensor_tensor(out=TMP, in0=TMP, scalar=0.0, in1=ATT8.unsqueeze(1).to_broadcast([P, CH, D]),
                                                op0=ALU.max, op1=ALU.mult))
                    join()
                    link(v.tensor_reduce(SELF[:, T, 0:H], hc(TMP), AX.X, ALU.add))
                    join()
                    for side in range(2):
                        link(v.tensor_tensor(SELF[:, T, 0:H], SELF[:, T, 0:H], XLR[:, T, side, D:D + H], ALU.add))
                        join()
                v.sem_inc(sem("g_node"), 1)

                def selector(j, s):
                    v.tensor_scalar(PM2[:, s, :], iota_row[:, :], DR[:, bass.ds(j, 1)], None, ALU.is_equal).then_inc(sem("ga_sel"), 1)

                for s in range(UNR):
                    selector(s, s)
                v.sem_inc(sem("ga_lg"), HALF)
                with v.Fori(0, TURNS) as k:
                    for h in range(2):
                        def finish(i):
                            s = h * HALF + i
                            v.wait_ge(sem("ga_lk"), (k * UNR + s) * 2 + 2 + since(g, "a_lk"))
                            v.tensor_tensor(LGT[:, bass.ds(k * UNR + s, 1), 0:H].rearrange("p o h -> p (o h)"), REL[:, s, 0:H],
                                            PS[:, 4 + i, D:D + H], ALU.add).then_inc(sem("ga_lg"), 1)
                        for i in range(HALF):
                            s = h * HALF + i
                            v.wait_ge(sem("ga_pair"), k * UNR + (s + UNR + 1) + since(g, "a_pair"))
                            v.scalar_tensor_tensor(out=GX[:, s, :], in0=PS[:, 4 + i, 0:D], scalar=0.0, in1=ATT8,
                                                   op0=ALU.max, op1=ALU.mult).then_inc(sem("ga_lk"), 1)
                            if i:
                                finish(i - 1)
                            v.wait_ge(sem("ga_tp"), k * UNR + (s + 1) + since(g, "a_tp"))
                            selector(k * UNR + (s + AHEAD), s)
                            v.wait_ge(sem("ga_lk"), (k * UNR + s) * 2 + 1 + since(g, "a_lk"))
                            v.tensor_reduce(REL[:, s, 0:H], GX[:, s, :].rearrange("p (h c) -> p h c", h=H), AX.X,
                                            ALU.add).then_inc(sem("ga_lk"), 1)
                        finish(HALF - 1)
                v.wait_ge(sem("ga_lg"), PAIRS + HALF + since(g, "a_lg"))
                v.sem_inc(sem("g_logits"), 1)

                for g4 in range(GROUPS):
                    v.wait_ge(sem("g_rows"), g4 + 1 + since(g, "_rows"))
                    link(v.tensor_tensor(ROWA[:, g4, 0:H, :], PS[0:RPG, g4, 0:H * P].rearrange("p (h e) -> p h e", h=H),
                                         V_ROW[:, g4, :].unsqueeze(1).to_broadcast([RPG, H, P]), ALU.add))
                join()
                for g4 in range(GROUPS):
                    for h in range(H):
                        link(v.tensor_tensor_scan(out=ROWB[:, g4, h, :], data0=F_ROW[:, g4, :], data1=ROWA[:, g4, h, :],
                                                  initial=NEG, op0=ALU.add, op1=ALU.max))
                        link(v.tensor_tensor_scan(out=ROWC[:, g4, h, ::-1], data0=E_ROW[:, g4, ::-1], data1=ROWA[:, g4, h, ::-1],
                                                  initial=NEG, op0=ALU.add, op1=ALU.max))
                join()
                v.sem_inc(sem("g_scans"), 1)
                v.wait_ge(sem("g_ends"), 1 + since(g, "_ends"))
                for i in range(2):
                    link(v.memset(ROWH[i][:, :], NEG))
                join()
                link(v.tensor_tensor_scan(out=ROWH[0][0:H, 1:PAIRS + 1], data0=row_start[0:H, :], data1=PS[0:H, 4, 0:PAIRS],
                                          initial=NEG, op0=ALU.add, op1=ALU.max))
                link(v.tensor_tensor_scan(out=ROWH[1][0:H, PAIRS - 1::-1], data0=row_end[0:H, ::-1],
                                          data1=PS[0:H, 5, PAIRS - 1::-1], initial=NEG, op0=ALU.add, op1=ALU.max))
                join()
                v.sem_inc(sem("g_carry"), 1)
                link(v.tensor_tensor(ROWB[:, :, 0:H, :], ROWB[:, :, 0:H, :], ROWC[:, :, 0:H, :], ALU.max))
                v.wait_ge(sem("g_back"), 1 + since(g, "_back"))
                for i in range(2):
                    link(v.tensor_copy(COLH[:, i, :, 0:H], PS[0:RPG, 6 + i, 0:GROUPS * H].rearrange("p (g h) -> p g h", g=GROUPS)))
                join()
                for i, mask in enumerate((LEAD, TRAIL)):
                    for g4 in range(GROUPS):
                        for h in range(H):
                            link(v.scalar_tensor_tensor(out=ROWB[:, g4, h, :], in0=mask[:, g4, :], scalar=COLH[:, i, g4, h:h + 1],
                                                        in1=ROWB[:, g4, h, :], op0=ALU.add, op1=ALU.max))
                    join()
                link(v.tensor_tensor(ROWA[:, :, 0:H, :], ROWA[:, :, 0:H, :], ROWB[:, :, 0:H, :], ALU.subtract))
                for g4 in range(GROUPS):
                    link(v.tensor_scalar(ROWC[:, g4, 0, :], E_ROW[:, g4, :], 1.0 / NEG, None, ALU.mult))
                join()
                for h in range(H - 1, -1, -1):
                    link(v.tensor_tensor(ROWC[:, :, h, :], ROWC[:, :, 0, :], ROWB[:, :, h, :], ALU.mult))
                    join()
                v.sem_inc(sem("g_shift"), 1)
                v.wait_ge(sem("g_cols"), 1 + since(g, "_cols"))
                for h in range(H):
                    link(v.tensor_copy(EXM[:, :, 0:W][:, :, h], PS[:, h, 0:PAIRS]))
                    link(v.tensor_copy(EXM[:, :, 0:W][:, :, H + h], PS[:, 4 + h, 0:PAIRS]))
                link(v.tensor_copy(EXM[:, :, 0:W][:, :, 2 * H], EN[:, :]))
                link(v.memset(ACC, 0.0))
                join()
                v.sem_inc(sem("g_exm"), 1)

                def pick(j, s):
                    v.tensor_scalar(PM2[:, s, :], iota_row[:, :], DR[:, bass.ds(j, 1)], None, ALU.is_equal).then_inc(sem("gb_sel"), 1)

                gath0 = (LAYERS + 2 * g["no"] + 1) * 16 * TURNS
                for i in range(HALF):
                    pick(i, i)
                v.sem_inc(sem("gb_acc"), HALF)
                with v.Fori(0, TURNS) as k:
                    _, blk = nc.values_load_multi_w_load_instructions(
                        brow[0:1, bass.ds(k * UNR, UNR)], engines=[mybir.EngineType.DVE], min_val=0, max_val=NT - 1,
                        skip_runtime_bounds_check_because="block numbers are counts of up to NT - 1 thresholds")
                    for h in range(2):
                        for i in range(HALF):
                            s = h * HALF + i
                            v.wait_ge(sem(f"gath{s}"), k * 16 + (gath0 + 16))
                            v.wait_ge(sem("gb_pair"), k * UNR + (s + 1) + since(g, "b_pair"))
                            w = EXM[:, bass.ds(k * UNR + s, 1), 0:H].rearrange("p o h -> p (o h)")
                            v.tensor_tensor(GX[:, s, :].rearrange("p (h c) -> p h c", h=H),
                                            G2[:, s, 0:D].rearrange("p (h c) -> p h c", h=H),
                                            w.unsqueeze(2).to_broadcast([P, H, C]), ALU.mult).then_inc(sem("gb_gx"), 1)
                            v.wait_ge(sem("gb_pair"), k * UNR + (s + HALF + 1) + since(g, "b_pair"))
                            pick(k * UNR + (s + HALF), (s + HALF) % UNR)
                        for i in range(HALF):
                            s = h * HALF + i
                            v.wait_ge(sem("gb_pair"), k * UNR + (s + UNR + 1) + since(g, "b_pair"))
                            v.wait_ge(sem("gb_acc"), k * UNR + (s + HALF) + since(g, "b_acc"))
                            at = ACC[:, bass.ds(blk[s], 1), 0:D + W].rearrange("p o n -> p (o n)")
                            v.tensor_tensor(at, at, PS[:, i, 0:D + W], ALU.add).then_inc(sem("gb_acc"), 1)
                v.wait_ge(sem("gb_acc"), PAIRS + HALF + since(g, "b_acc"))

                mt, ea, eb, dn = [x[:, :, 0:H] for x in NODE]
                den, mm_, pr = ACC[:, :, D:D + H], ACC[:, :, D + H:D + 2 * H], ACC[:, :, D + 2 * H:D + 2 * H + 1]
                slf = SELF[:, :, 0:H]
                link(v.tensor_scalar(dn, pr.to_broadcast([P, NT, H]), -NEG, NEG, ALU.mult, ALU.add))
                join()
                link(v.tensor_tensor(ea, dn, mm_, ALU.add))
                join()
                link(v.tensor_tensor(mt, ea, slf, ALU.max))
                join()
                link(v.tensor_tensor(ea, ea, mt, ALU.subtract))
                link(v.tensor_tensor(eb, slf, mt, ALU.subtract))
                join()
                v.sem_inc(sem("g_sh2"), 1)
                v.wait_ge(sem("g_e2"), 2 + since(g, "_e2"))
                link(v.tensor_tensor(dn, den, ea, ALU.mult))
                join()
                link(v.tensor_tensor(dn, dn, eb, ALU.add))
                join()
                link(v.reciprocal(mt, dn))
                join()
                link(v.tensor_tensor(ea, ea, mt, ALU.mult))
                link(v.tensor_tensor(eb, eb, mt, ALU.mult))
                join()
                num = ACC[:, :, 0:D]
                own = XLR[:, :, 0, 0:D]
                for c in range(NCH):
                    T = slice(c * CH, (c + 1) * CH)
                    wide = lambda x: x[:, T, :].unsqueeze(3).to_broadcast([P, CH, H, C])
                    link(v.tensor_tensor(hc(num[:, T, :]), hc(num[:, T, :]), wide(ea), ALU.mult))
                    link(v.tensor_tensor(hc(own[:, T, :]), hc(own[:, T, :]), wide(eb), ALU.mult))
                    join()
                    link(v.tensor_tensor(num[:, T, :], num[:, T, :], own[:, T, :], ALU.add))
                    join()
                    link(v.tensor_tensor(num[:, T, :], num[:, T, :], BIAS.unsqueeze(1).to_broadcast([P, CH, D]), ALU.add))
                    join()
                    if g["last"]:
                        link(v.tensor_tensor(X[:, T, :], X[:, T, :], num[:, T, :], ALU.add))
                    else:
                        link(v.tensor_scalar(YNG[:, T, :], num[:, T, :], 0.0, None, ALU.min))
                        join()
                        v.sem_inc(sem("g_neg"), 1)
                        v.wait_ge(sem("g_eneg"), c + 1 + since(g, "_eneg"))
                        link(v.tensor_scalar(YNG[:, T, :], YNG[:, T, :], 1.0, None, ALU.subtract))
                        join()
                        link(v.scalar_tensor_tensor(out=YNG[:, T, :], in0=num[:, T, :], scalar=0.0, in1=YNG[:, T, :],
                                                    op0=ALU.max, op1=ALU.add))
                    join()

            link(v.memset(DR[:, :], 0.0))
            link(v.memset(WE[:, :], 0.0))
            link(v.memset(eps[:, :], 1e-5))
            v.wait_ge(sem("iotas"), 3)
            link(v.tensor_copy(iota_row[:, :], iota_i))
            link(v.tensor_copy(jrow, jrow_i))
            link(v.tensor_copy(jcol, jcol_i))
            link(v.memset(bacc[0], 0.0))
            link(v.memset(cnt, 0.0))
            v.wait_ge(sem("dst_in"), 16)
            link(v.tensor_copy(dst_f, dst_i))
            join()
            for b in range(NB):
                link(v.tensor_scalar(cnt_junk, dst_f, float(P * (b + 1)), None, ALU.is_lt, ALU.add,
                                     accum_out=cnt[0:SPLIT, b:b + 1]))
                join()
            v.sem_inc(sem("cnt"), 1)
            v.wait_ge(sem("cnt_mm"), 1)
            link(v.tensor_copy(tot_i, PS[:, 0, 0:NB]))
            join()
            link(v.tensor_scalar(tot_i, tot_i, 7, None, ALU.arith_shift_right))
            join()
            link(v.tensor_copy(thr, tot_i))
            join()
            link(v.tensor_tensor(thr, thr, iota_row[:, 0:NB], ALU.add))
            join()
            for b in range(NB):
                link(v.scalar_tensor_tensor(out=bacc[(b + 1) % 2], in0=jrow, scalar=thr[:, b:b + 1],
                                            in1=bacc[b % 2], op0=ALU.is_gt, op1=ALU.add))
                join()
            link(v.tensor_copy(brow[0:1, :], bacc[NB % 2][0:1, :]))
            link(v.tensor_tensor(cmp, jcol.unsqueeze(2).to_broadcast([RPG, GROUPS, NB]),
                                 thr[0:RPG, :].unsqueeze(1).to_broadcast([RPG, GROUPS, NB]), ALU.is_gt))
            join()
            link(v.tensor_reduce(bcol, cmp, AX.X, ALU.add))
            join()
            link(v.tensor_tensor(tcol, jcol, bcol, ALU.subtract))
            link(v.tensor_scalar(blo, bcol, float(P), None, ALU.mult))
            join()
            v.tensor_copy(tcol_i, tcol).then_inc(sem("tcol"), 1)
            v.wait_ge(sem("rowmeta"), 16 * 2 * GROUPS)
            link(v.tensor_copy(rowf, rowi))
            join()
            sec = lambda s: rowf[:, :, s * P:(s + 1) * P]
            for g in range(GROUPS):
                link(v.tensor_scalar(dr_row[:, g, :], sec(1)[:, g, :], blo[:, g:g + 1], None, ALU.subtract))
            join()
            link(v.tensor_scalar(V_ROW[:, :, :], dr_row, 0.0, None, ALU.is_ge))
            link(v.tensor_scalar(t0_row, dr_row, float(P), None, ALU.is_lt))
            link(v.tensor_tensor(F_ROW[:, :, :], sec(0), sec(1), ALU.not_equal))
            link(v.tensor_tensor(E_ROW[:, :, :], sec(2), sec(1), ALU.not_equal))
            join()
            link(v.tensor_tensor(V_ROW[:, :, :], V_ROW[:, :, :], t0_row, ALU.mult))
            join()
            link(v.tensor_tensor(F_ROW[:, :, :], F_ROW[:, :, :], V_ROW[:, :, :], ALU.mult))
            link(v.tensor_tensor(E_ROW[:, :, :], E_ROW[:, :, :], V_ROW[:, :, :], ALU.mult))
            join()
            v.sem_inc(sem("row_flags"), 1)
            v.wait_ge(sem("meta_tp"), 4)
            link(v.tensor_copy(DR[:, 0:PAIRS], PS[:, 1, 0:PAIRS]))
            link(v.tensor_copy(SRC[:, :], PS[:, 2, 0:PAIRS]))
            link(v.tensor_copy(WE[:, 0:PAIRS], PS[:, 3, 0:PAIRS]))
            link(v.tensor_copy(EN[:, :], PS[:, 4, 0:PAIRS]))
            link(v.tensor_copy(DR[:, PAIRS:], PS[:, 1, 0:AHEAD]))
            link(v.tensor_copy(WE[:, PAIRS:], PS[:, 3, 0:AHEAD]))
            for g in range(GROUPS):
                link(v.tensor_tensor_scan(out=LEAD[:, g, :], data0=F_ROW[:, g, :], data1=F_ROW[:, g, :],
                                          initial=0.0, op0=ALU.max, op1=ALU.max))
                link(v.tensor_tensor_scan(out=TRAIL[:, g, ::-1], data0=E_ROW[:, g, ::-1], data1=E_ROW[:, g, ::-1],
                                          initial=0.0, op0=ALU.max, op1=ALU.max))
            join()
            for buf in (LEAD, TRAIL, F_ROW, E_ROW):
                link(v.tensor_scalar(buf[:, :, :], buf[:, :, :], NEG, None, ALU.mult))
            link(v.tensor_scalar(V_ROW[:, :, :], V_ROW[:, :, :], -NEG, NEG, ALU.mult, ALU.add))
            join()
            link(v.tensor_copy(any_start, LEAD[:, :, P - 1:P].to_broadcast([RPG, GROUPS, HEADS])))
            link(v.tensor_copy(any_end, TRAIL[:, :, 0:1].to_broadcast([RPG, GROUPS, HEADS])))
            join()
            v.sem_inc(sem("row_any"), 1)
            v.wait_ge(sem("any_tp"), 1)
            link(v.tensor_copy(row_start[:, :], PS[0:HEADS, 5, 0:PAIRS]))
            link(v.tensor_copy(row_end[:, :], PS[0:HEADS, 6, 0:PAIRS]))
            join()
            v.sem_inc(sem("meta_end"), 1)

            v.wait_ge(sem("x_in"), 32)
            for t in range(NT):
                link(v.bn_stats(st[:, t, :], X[:, t, :]))
            join()
            for t in range(NT):
                link(v.bn_aggr(mv[:, t, :], st[:, t, :]))
            join()
            v.sem_inc(sem("ln0_mv"), 1)
            v.wait_ge(sem("ln0_std"), 1)
            link(v.reciprocal(rstd[:, :], std[:, :]))
            join()
            for t in range(NT):
                v.tensor_scalar(HN[:, t, :], X[:, t, :], mv[:, t, 0:1], rstd[:, t:t + 1], ALU.subtract, ALU.mult).then_inc(sem("ln0_y"), 1)
            v.wait_ge(sem("wg_in"), 64)
            v.tensor_tensor(b_rz, b_raw[:, 0:4], b_raw[:, 6:10], ALU.add).then_inc(sem("b_rz"), 1)
            v.sem_inc(sem("gru_credit"), 1)
            v.sem_inc(sem("agg_free"), HALF)
            v.sem_inc(sem("nn_read"), 2)
            v.sem_inc(sem("h_new"), 2)

            def selectors(j, first):
                for i in range(HALF):
                    s = first + i
                    v.wait_ge(sem("pair_used"), j[1] + (i + 1))
                    v.tensor_scalar(PM[:, s, :], iota_row[:, :], DR[:, bass.ds(j[0] + i, 1)],
                                    WE[:, bass.ds(j[0] + i, 1)], ALU.is_equal, ALU.mult).then_inc(sem("sel_in"), 1)

            join()
            v.wait_ge(sem("pair_used"), UNR)
            selectors((0, 0), 0)
            with v.Fori(0, LAYERS) as l:
                v.wait_ge(sem("h_new"), l * (4 * NCH) + 2)
                v.memset(AG, 0.0).then_inc(sem("ag_zero"), 1)
                v.wait_ge(sem("ag_zero"), l + 1)
                v.sem_inc(sem("v_passed"), 1)
                with v.Fori(0, TURNS) as k:
                    _, blk = nc.values_load_multi_w_load_instructions(
                        brow[0:1, bass.ds(k * UNR, UNR)], engines=[mybir.EngineType.DVE], min_val=0, max_val=NT - 1,
                        skip_runtime_bounds_check_because="block numbers are counts of up to NT - 1 thresholds")
                    for h in range(2):
                        selectors((k * UNR + (h + 1) * HALF, l * PAIRS + (k * UNR + (h + 1) * HALF)), (1 - h) * HALF)
                        for i in range(HALF):
                            s = h * HALF + i
                            done = l * PAIRS + (k * UNR + s)
                            v.wait_ge(sem("pair_used"), done + (UNR + 1))
                            v.wait_ge(sem("agg_free"), done + HALF)
                            dst_v = AG[:, :, bass.ds(blk[s] * P, P)]
                            v.tensor_tensor(dst_v, dst_v, PS[:, i, 0:D].rearrange("p (c n) -> p c n", c=2),
                                            ALU.add).then_inc(sem("agg_free"), 1)
                with v.Fori(0, NCH) as c:
                    for u, (o, n) in enumerate(SUBS):
                        q = l * (4 * NCH) + (c * 4 + 2 * u)
                        g = l * (12 * NCH) + (c * 12 + 6 * u)
                        B = 4
                        for f in range(2):
                            v.wait_ge(sem("rz_done"), q + (f + 3))
                            v.scalar_tensor_tensor(out=gbuf[:, 2, f, 0:n], in0=PS[:, B * f + 3, 0:n],
                                                   scalar=b_raw[:, 10 + f:11 + f], in1=gbuf[:, 0, f, 0:n],
                                                   op0=ALU.add, op1=ALU.mult).then_inc(sem("gru_link"), 1)
                        for f in range(2):
                            v.wait_ge(sem("gru_link"), g + (f + 1))
                            v.tensor_tensor(gbuf[:, 2, f, 0:n], gbuf[:, 2, f, 0:n], PS[:, B * f + 2, 0:n],
                                            ALU.add).then_inc(sem("nn_read"), 1)
                        for f in range(2):
                            v.wait_ge(sem("n_done"), q + (f + 1))
                            v.tensor_tensor(gbuf[:, 2, f, 0:n], HT[:, f, bass.ds(c * CHN + o, n)],
                                            gbuf[:, 3, f, 0:n], ALU.subtract).then_inc(sem("gru_link"), 1)
                        for f in range(2):
                            v.wait_ge(sem("gru_link"), g + (f + 3))
                            v.tensor_tensor(gbuf[:, 2, f, 0:n], gbuf[:, 2, f, 0:n], gbuf[:, 1, f, 0:n],
                                            ALU.mult).then_inc(sem("gru_link"), 1)
                        v.wait_ge(sem("gru_mm"), q + 2)
                        for f in range(2):
                            v.wait_ge(sem("gru_link"), g + (f + 5))
                            v.tensor_tensor(HT[:, f, bass.ds(c * CHN + o, n)], gbuf[:, 2, f, 0:n],
                                            gbuf[:, 3, f, 0:n], ALU.add).then_inc(sem("h_new"), 1)
            v.wait_ge(sem("tp_free"), LAYERS * NT + CH)
            link(v.tensor_tensor(X[:, :, :], X[:, :, :], HN, ALU.add))
            join()
            v.wait_ge(sem("table_in"), 16 * NCH * (LAYERS + 1))
            v.sem_inc(sem("x1"), 1)
            ffn_dve(FFN0)
            gat_dve(GAT1)
            gat_dve(GAT2)
            ffn_dve(FFN1)
            v.sem_inc(sem("x4"), 1)

        @block.scalar
        def _(act):
            def norm_std(tag):
                act.wait_ge(sem(tag + "_mv"), 1)
                nc.scalar.activation(std[:, :], mv[:, :, 1], ACT.Sqrt, bias=eps[:, :]).then_inc(sem(tag + "_std"), 1)

            def feature_major(tag, dst, affine=False):
                for t in range(NT):
                    act.wait_ge(sem(tag + "_tp"), t + 1)
                    if affine:
                        for c in range(2):
                            last = nc.scalar.activation(dst[:, c, t * P:(t + 1) * P], PS[:, t % 4, c * P:(c + 1) * P], ACT.Identity,
                                                        scale=GBT[:, c:c + 1], bias=GBT[:, 2 + c:3 + c])
                        last.then_inc(sem(tag + "_cp"), 1)
                    else:
                        nc.scalar.copy(dst[:, :, t * P:(t + 1) * P],
                                       PS[:, t % 4, 0:D].rearrange("p (c n) -> p c n", c=2)).then_inc(sem(tag + "_cp"), 1)

            def ffn_act(f):
                t, Fh, E = f["tag"], f["Fh"], f["E"]
                MF = Fh // P
                EC = E + (1 if f["shared"] else 0)
                norm_std(t + "n")
                if not f["shared"]:
                    norm_std(t + "m")
                    act.wait_ge(sem(t + "_small"), 80)
                feature_major(t, YT, affine=not f["shared"])
                act.wait_ge(sem(t + "_d"), 1)
                nc.scalar.activation(TOP[6], TOP[3], ACT.Exp).then_inc(sem(t + "_ed"), 1)
                for q in range(7):
                    n = min(4, NT - 4 * q) * P
                    act.wait_ge(sem(t + "_mtp"), q + 1)
                    nc.scalar.copy(MSKT[0:EC, q * 512:q * 512 + n], PS[0:EC, q, 0:n]).then_inc(sem(t + "_mcp"), 1)
                act.sem_inc(sem(t + "_hid"), 2)

                def hidden(e, w, wcount):
                    act.wait_ge(sem(f"{t}_w{w}"), wcount)
                    act.sem_inc(sem("act_passed"), 1)
                    with act.Fori(0, NCH) as c:
                        for u, (o, n) in enumerate(SUBS):
                            q = (e * NCH + c) * 2 + u
                            act.wait_ge(sem(t + "_y"), (e * NCH + c) * CH + (2 * NT - CH + (3, 5)[u]))
                            for m in range(MF):
                                act.wait_ge(sem(t + "_hmm"), q * MF + (m + 1))
                                nc.scalar.activation(HID[u][:, m, 0:n], PS[:, m % 2, 0:n], ACT.Gelu,
                                                     bias=B1B[w][:, m:m + 1]).then_inc(sem(t + "_hid"), 1)
                first = 0
                if f["shared"]:
                    hidden(0, 1, 48)
                    first = 1
                with act.Fori(0, E // 2) as e:
                    for w in range(2):
                        hidden(e * 2 + (w + first), w, e * 48 + (48 + (48 if first and w == 1 else 0)))

            def gat_act(g):
                t, H = g["tag"], g["H"]
                if not g["last"]:
                    norm_std(t + "n")
                feature_major(t, YTG)
                for i in range(NT):
                    act.wait_ge(sem("g_xmm"), i + 1 + since(g, "_xmm"))
                    nc.scalar.copy(XLR[:, i, :, 0:D], PS[:, 4 + i % 4, :].rearrange("p (s n) -> p s n", s=2)).then_inc(sem("g_xlr"), 1)
                for i in range(HALF):
                    act.wait_ge(sem("ga_tp"), i + 1 + since(g, "a_tp"))
                    nc.scalar.copy(PT2[:, i, :], PS[:, i, 0:P]).then_inc(sem("ga_pt"), 1)
                with act.Fori(0, TURNS) as k:
                    for s in range(UNR):
                        d = (s + HALF) % UNR
                        act.wait_ge(sem("ga_tp"), k * UNR + (s + HALF + 1) + since(g, "a_tp"))
                        act.wait_ge(sem("ga_pair"), k * UNR + (s + HALF + 1) + since(g, "a_pair"))
                        nc.scalar.copy(PT2[:, d, :], PS[:, s % HALF, 0:P]).then_inc(sem("ga_pt"), 1)
                act.wait_ge(sem("g_shift"), 1 + since(g, "_shift"))
                nc.scalar.activation(ROWA[:, :, 0:H, :], ROWA[:, :, 0:H, :], ACT.Exp).then_inc(sem("g_ex"), 1)
                act.wait_ge(sem("g_sh2"), 1 + since(g, "_sh2"))
                for x in NODE[1:3]:
                    nc.scalar.activation(x[:, :, 0:H], x[:, :, 0:H], ACT.Exp).then_inc(sem("g_e2"), 1)
                if not g["last"]:
                    for c in range(NCH):
                        act.wait_ge(sem("g_neg"), c + 1 + since(g, "_neg"))
                        part = YNG[:, c * CH:(c + 1) * CH, :]
                        nc.scalar.activation(part, part, ACT.Exp).then_inc(sem("g_eneg"), 1)
            act.wait_ge(sem("ln0_mv"), 1)
            nc.scalar.activation(std[:, :], mv[:, :, 1], ACT.Sqrt, bias=eps[:, :]).then_inc(sem("ln0_std"), 1)
            for w, dstw in enumerate((WIT, WHT)):
                for kc in range(2):
                    for part in range(2):
                        q = w * 4 + kc * 2 + part
                        act.wait_ge(sem("wt_tp"), q + 1)
                        n = (512, 256)[part]
                        nc.scalar.copy(dstw[:, kc, part * 512:part * 512 + n], PS[:, q, 0:n]).then_inc(sem("wt_cp"), 1)
            for t in range(NT):
                act.wait_ge(sem("t0_tp"), t + 1)
                nc.scalar.copy(HT[:, :, t * P:(t + 1) * P], PS[:, t % 8, 0:D].rearrange("p (c n) -> p c n", c=2)).then_inc(sem("t0_cp"), 1)
            act.wait_ge(sem("b_rz"), 1)
            act.wait_ge(sem("gru_credit"), 1)
            act.sem_inc(sem("rz_done"), 2)
            act.wait_ge(sem("rz_done"), 2)
            act.sem_inc(sem("tp_free"), CH)
            act.wait_ge(sem("tp_free"), CH)
            act.sem_inc(sem("fold_free"), 1)
            with act.Fori(0, LAYERS) as l:
                act.wait_ge(sem("fold_mm"), l * 3 + 1)
                nc.scalar.copy(WLT.rearrange("p a b -> p (a b)"), PS[:, 4, :]).then_inc(sem("wlt"), 1)
                act.wait_ge(sem("h_new"), l * (4 * NCH) + 2)
                for kc in range(2):
                    act.wait_ge(sem("fold_mm"), l * 3 + (kc + 2))
                    b0, b1 = ((5, 6), (7, 4))[kc]
                    nc.scalar.copy(WI[:, kc, 0:512], PS[:, b0, :]).then_inc(sem("wi"), 1)
                    nc.scalar.copy(WI[:, kc, 512:GD], PS[:, b1, 0:256]).then_inc(sem("wi"), 1)
                act.wait_ge(sem("wi"), l * 4 + 4)
                act.sem_inc(sem("fold_free"), 1)
                with act.Fori(0, NCH) as c:
                    for u, (o, n) in enumerate(SUBS):
                        q = l * (4 * NCH) + (c * 4 + 2 * u)
                        for f in range(2):
                            act.wait_ge(sem("gru_mm"), q + (f + 1))
                            act.wait_ge(sem("h_new"), q + (f + 1))
                            nc.scalar.activation(gbuf[:, 0, f, 0:n], PS[:, 4 * f, 0:n], ACT.Sigmoid, bias=b_rz[:, f:f + 1])
                            nc.scalar.activation(gbuf[:, 1, f, 0:n], PS[:, 4 * f + 1, 0:n], ACT.Sigmoid,
                                                 bias=b_rz[:, 2 + f:3 + f]).then_inc(sem("rz_done"), 1)
                        for f in range(2):
                            act.wait_ge(sem("nn_read"), q + (f + 3))
                            nc.scalar.activation(gbuf[:, 3, f, 0:n], gbuf[:, 2, f, 0:n], ACT.Tanh,
                                                 bias=b_raw[:, 4 + f:5 + f]).then_inc(sem("n_done"), 1)
                act.wait_ge(sem("table_in"), l * (16 * NCH) + 16 * NCH)
                for t in range(NT):
                    act.wait_ge(sem("tp_done"), l * NT + (t + 1))
                    nc.scalar.copy(HN[:, t, :], PS[:, t % CH, 0:D]).then_inc(sem("tp_free"), 1)
            act.wait_ge(sem("x1"), 1)
            ffn_act(FFN0)
            gat_act(GAT1)
            gat_act(GAT2)
            ffn_act(FFN1)

        @block.tensor
        def _(pe):
            mm = nc.tensor.matmul
            tp = nc.tensor.transpose
            def to_feature_major(tag, src):
                for t in range(NT):
                    if t >= 4:
                        pe.wait_ge(sem(tag + "_cp"), t - 3)
                    tp(PS[:, t % 4, 0:P], src[:, t, 0:P], ident[:, :])
                    tp(PS[:, t % 4, P:D], src[:, t, P:D], ident[:, :]).then_inc(sem(tag + "_tp"), 1)
                pe.wait_ge(sem(tag + "_cp"), NT)

            def ffn_pe(f):
                t, Fh, E = f["tag"], f["Fh"], f["E"]
                MF = Fh // P
                EC = E + (1 if f["shared"] else 0)
                pe.sem_inc(sem(t + "_y"), 2 * NT)
                pe.wait_ge(sem(t + "_yn"), 1)
                to_feature_major(t, YN)
                pe.wait_ge(sem(t + "_small"), 48 if f["shared"] else 80)
                for i in range(NT):
                    mm(PS[:, 7, i * E:(i + 1) * E], YT[:, 0, i * P:(i + 1) * P], WRB[:, 0, :], start=True, stop=False)
                    last = mm(PS[:, 7, i * E:(i + 1) * E], YT[:, 1, i * P:(i + 1) * P], WRB[:, 1, :], start=False, stop=True)
                last.then_inc(sem(t + "_gate"), 1)
                pe.wait_ge(sem(t + "_msk"), 1)
                for q in range(7):
                    for i in range(4 * q, min(4 * q + 4, NT)):
                        last = tp(PS[0:EC, q, (i % 4) * P:(i % 4 + 1) * P], MSK[:, i, 0:EC], ident[:, :])
                    last.then_inc(sem(t + "_mtp"), 1)
                pe.wait_ge(sem(t + "_mcp"), 7)
                for i in range(NT):
                    if i >= CH:
                        pe.wait_ge(sem(t + "_b2free"), i - CH + 1)
                    mm(PS[:, 3 + i % CH, 0:D], MSKT[0:EC, i * P:(i + 1) * P], B2B[0:EC, :], start=True, stop=True).then_inc(sem(t + "_b2"), 1)
                pe.wait_ge(sem(t + "_b2free"), NT)

                def expert(e, w, wcount):
                    pe.wait_ge(sem(f"{t}_w{w}"), wcount)
                    pe.sem_inc(sem("pe_passed"), 1)
                    with pe.Fori(0, NCH) as c:
                        for u, (o, n) in enumerate(SUBS):
                            q = (e * NCH + c) * 2 + u
                            at = bass.ds(c * CHN + o, n)
                            for m in range(MF):
                                pe.wait_ge(sem(t + "_hid"), q * MF + (m + 1))
                                mm(PS[:, m % 2, 0:n], W1B[w][:, 0, m * P:(m + 1) * P], YT[:, 0, at], start=True, stop=False)
                                mm(PS[:, m % 2, 0:n], W1B[w][:, 1, m * P:(m + 1) * P], YT[:, 1, at], start=False, stop=True).then_inc(sem(t + "_hmm"), 1)
                            pe.wait_ge(sem(t + "_hid"), q * MF + (MF + 2))
                            for i in range(o // P, (o + n) // P):
                                pe.wait_ge(sem(t + "_yfree"), (e * NCH + c) * CH + (i + 1))
                                for m in range(MF):
                                    last = mm(PS[:, 3 + i, 0:D], HID[u][:, m, i * P - o:(i + 1) * P - o], W2B[w][:, m, :],
                                              start=m == 0, stop=m == MF - 1)
                                last.then_inc(sem(t + "_y"), 1)
                first = 0
                if f["shared"]:
                    expert(0, 1, 48)
                    first = 1
                with pe.Fori(0, E // 2) as e:
                    for w in range(2):
                        expert(e * 2 + (w + first), w, e * 48 + (48 + (48 if first and w == 1 else 0)))

            def gat_pe(g):
                t, H = g["tag"], g["H"]
                W = 2 * H + 1
                pe.wait_ge(sem("g_yn"), 1 + since(g, "_yn"))
                to_feature_major(t, YNG)
                pe.wait_ge(sem("g_w"), 64 + since(g, "_w"))
                for i in range(NT):
                    if i >= 4:
                        pe.wait_ge(sem("g_xlr"), i - 3 + since(g, "_xlr"))
                    mm(PS[:, 4 + i % 4, :], YTG[:, 0, i * P:(i + 1) * P], WLR[:, 0, :], start=True, stop=False)
                    mm(PS[:, 4 + i % 4, :], YTG[:, 1, i * P:(i + 1) * P], WLR[:, 1, :], start=False, stop=True).then_inc(sem("g_xmm"), 1)
                pe.wait_ge(sem("g_node"), 1 + since(g, "_node"))
                for i in range(HALF):
                    pe.wait_ge(sem("ga_sel"), i + 1 + since(g, "a_sel"))
                    tp(PS[:, i, 0:P], PM2[:, i, :], ident[:, :]).then_inc(sem("ga_tp"), 1)
                gath0 = (LAYERS + 2 * g["no"]) * 16 * TURNS
                with pe.Fori(0, TURNS) as k:
                    _, blk = nc.values_load_multi_w_load_instructions(
                        brow[0:1, bass.ds(k * UNR, UNR)], engines=[mybir.EngineType.PE], min_val=0, max_val=NT - 1,
                        skip_runtime_bounds_check_because="block numbers are counts of up to NT - 1 thresholds")
                    for h in range(2):
                        for i in range(HALF):
                            s = h * HALF + i
                            pe.wait_ge(sem("ga_sel"), k * UNR + (s + HALF + 1) + since(g, "a_sel"))
                            pe.wait_ge(sem("ga_pt"), k * UNR + (s + 1) + since(g, "a_pt"))
                            tp(PS[:, i, 0:P], PM2[:, (s + HALF) % UNR, :], ident[:, :]).then_inc(sem("ga_tp"), 1)
                            pe.wait_ge(sem(f"gath{s}"), k * 16 + (gath0 + 16))
                            pe.wait_ge(sem("ga_lg"), k * UNR + (s + 1) + since(g, "a_lg"))
                            mm(PS[:, 4 + i, 0:D + H], ident[:, :], G2[:, s, 0:D + H], start=True, stop=False)
                            mm(PS[:, 4 + i, 0:D + H], PT2[:, s, :], XLR[:, bass.ds(blk[s], 1), 1, 0:D + H].rearrange("p o n -> p (o n)"),
                               start=False, stop=True).then_inc(sem("ga_pair"), 1)
                pe.wait_ge(sem("g_logits"), 1 + since(g, "_logits"))
                pe.wait_ge(sem("ga_pt"), PAIRS + HALF + since(g, "a_pt"))
                for g4 in range(GROUPS):
                    for h in range(H):
                        last = tp(PS[0:RPG, g4, h * P:(h + 1) * P], LGT[:, g4 * RPG:(g4 + 1) * RPG, h], ident[:, :])
                    last.then_inc(sem("g_rows"), 1)
                pe.wait_ge(sem("g_scans"), 1 + since(g, "_scans"))
                for b, buf, col in ((4, ROWB, P - 1), (5, ROWC, 0)):
                    for g4 in range(GROUPS):
                        last = tp(PS[0:H, b, g4 * RPG:(g4 + 1) * RPG], buf[:, g4, 0:H, col], ident[0:RPG, 0:RPG])
                last.then_inc(sem("g_ends"), 1)
                pe.wait_ge(sem("g_carry"), 1 + since(g, "_carry"))
                for i in range(2):
                    for g4 in range(GROUPS):
                        last = tp(PS[0:RPG, 6 + i, g4 * H:(g4 + 1) * H], ROWH[i][0:H, g4 * RPG + i:(g4 + 1) * RPG + i], ident[0:H, 0:H])
                last.then_inc(sem("g_back"), 1)
                pe.wait_ge(sem("g_ex"), 1 + since(g, "_ex"))
                for h in range(H):
                    for g4 in range(GROUPS):
                        tp(PS[:, h, g4 * RPG:(g4 + 1) * RPG], ROWA[:, g4, h, :], ident[0:RPG, 0:RPG])
                        last = tp(PS[:, 4 + h, g4 * RPG:(g4 + 1) * RPG], ROWC[:, g4, h, :], ident[0:RPG, 0:RPG])
                last.then_inc(sem("g_cols"), 1)
                pe.wait_ge(sem("g_exm"), 1 + since(g, "_exm"))
                with pe.Fori(0, TURNS) as k:
                    for h in range(2):
                        for i in range(HALF):
                            s = h * HALF + i
                            pe.wait_ge(sem("gb_gx"), k * UNR + (s + 1) + since(g, "b_gx"))
                            pe.wait_ge(sem("gb_sel"), k * UNR + (s + 1) + since(g, "b_sel"))
                            pe.wait_ge(sem("gb_acc"), k * UNR + (s + 1) + since(g, "b_acc"))
                            mm(PS[:, i, 0:D], PM2[:, s, :], GX[:, s, :], start=True, stop=True)
                            mm(PS[:, i, D:D + W], PM2[:, s, :], EXM[:, bass.ds(k * UNR + s, 1), 0:W].rearrange("p o n -> p (o n)"),
                               start=True, stop=True).then_inc(sem("gb_pair"), 1)
            pe.wait_ge(sem("id"), 2)
            pe.wait_ge(sem("ones"), 1)
            pe.wait_ge(sem("cnt"), 1)
            mm(PS[:, 0, 0:NB], ones[0:SPLIT, :], cnt[0:SPLIT, :], start=True, stop=True).then_inc(sem("cnt_mm"), 1)
            pe.wait_ge(sem("row_flags"), 1)
            for q, rows_of in enumerate((dr_row, rowf[:, :, 3 * P:4 * P], roww, E_ROW)):
                for g in range(GROUPS):
                    last = tp(PS[:, 1 + q, g * RPG:(g + 1) * RPG], rows_of[:, g, :], ident[0:RPG, 0:RPG])
                last.then_inc(sem("meta_tp"), 1)
            pe.wait_ge(sem("row_any"), 1)
            for b, any_of in ((5, any_start), (6, any_end)):
                for g in range(GROUPS):
                    last = tp(PS[0:HEADS, b, g * RPG:(g + 1) * RPG], any_of[:, g, :], ident[0:RPG, 0:RPG])
            last.then_inc(sem("any_tp"), 1)
            pe.wait_ge(sem("meta_end"), 1)
            pe.wait_ge(sem("wg_in"), 64)
            for w in range(2):
                raw = cut(arena, 1536 * w, (6, D))
                for kc in range(2):
                    for part in range(2):
                        for m in range((4, 2)[part]):
                            last = tp(PS[:, w * 4 + kc * 2 + part, m * P:(m + 1) * P],
                                      raw[:, part * 4 + m, kc * P:(kc + 1) * P], ident[:, :])
                        last.then_inc(sem("wt_tp"), 1)
            pe.wait_ge(sem("wt_cp"), 8)
            pe.wait_ge(sem("ln0_y"), NT)
            for t in range(NT):
                if t >= 8:
                    pe.wait_ge(sem("t0_cp"), t - 7)
                tp(PS[:, t % 8, 0:P], HN[:, t, 0:P], ident[:, :])
                tp(PS[:, t % 8, P:D], HN[:, t, P:D], ident[:, :]).then_inc(sem("t0_tp"), 1)
            pe.wait_ge(sem("t0_cp"), NT)
            with pe.Fori(0, LAYERS) as l:
                pe.wait_ge(sem("wl_in"), l * 16 + 16)
                pe.wait_ge(sem("tp_free"), l * NT + CH)
                for cc in range(2):
                    for kc in range(2):
                        last = tp(PS[:, 4, cc * D + kc * P:cc * D + (kc + 1) * P], WL[:, kc, cc * P:(cc + 1) * P], ident[:, :])
                last.then_inc(sem("fold_mm"), 1)
                pe.wait_ge(sem("wlt"), l + 1)
                for kc in range(2):
                    for b, (o, n) in zip(((5, 6), (7, 4))[kc], ((0, 512), (512, 256))):
                        for cc in range(2):
                            last = mm(PS[:, b, 0:n], WLT[:, cc, kc * P:(kc + 1) * P], WIT[:, cc, o:o + n],
                                      start=cc == 0, stop=cc == 1)
                    last.then_inc(sem("fold_mm"), 1)
                with pe.Fori(0, TURNS) as k:
                    for h in range(2):
                        for i in range(HALF):
                            s = h * HALF + i
                            j = l * PAIRS + (k * UNR + s)
                            pe.wait_ge(sem("sel_in"), j + 1)
                            pe.wait_ge(sem(f"gath{s}"), l * (16 * TURNS) + (k * 16 + 16))
                            pe.wait_ge(sem("agg_free"), j + 1)
                            mm(PS[:, i, 0:P], G[:, s, 0:P], PM[:, s, :], start=True, stop=True)
                            mm(PS[:, i, P:D], G[:, s, P:D], PM[:, s, :], start=True, stop=True).then_inc(sem("pair_used"), 1)
                pe.wait_ge(sem("agg_free"), l * PAIRS + (PAIRS + HALF))
                pe.wait_ge(sem("wi"), l * 4 + 4)
                pe.sem_inc(sem("pe_passed"), 1)
                with pe.Fori(0, NCH) as c:
                    for u, (o, n) in enumerate(SUBS):
                        for f in range(2):
                            q = l * (4 * NCH) + (c * 4 + (2 * u + f))
                            pe.wait_ge(sem("rz_done"), q + 1)
                            pe.wait_ge(sem("nn_read"), q + 1)
                            at = bass.ds(c * CHN + o, n)
                            for gate in range(2):
                                col = gate * D + f * P
                                b = 4 * f + gate
                                mm(PS[:, b, 0:n], WI[:, 0, col:col + P], AG[:, 0, at], start=True, stop=False)
                                mm(PS[:, b, 0:n], WI[:, 1, col:col + P], AG[:, 1, at], start=False, stop=False)
                                mm(PS[:, b, 0:n], WHT[:, 0, col:col + P], HT[:, 0, at], start=False, stop=False)
                                mm(PS[:, b, 0:n], WHT[:, 1, col:col + P], HT[:, 1, at], start=False, stop=True)
                            col = 2 * D + f * P
                            for w, src_t, b in ((WI, AG, 4 * f + 2), (WHT, HT, 4 * f + 3)):
                                mm(PS[:, b, 0:n], w[:, 0, col:col + P], src_t[:, 0, at], start=True, stop=False)
                                last = mm(PS[:, b, 0:n], w[:, 1, col:col + P], src_t[:, 1, at], start=False, stop=True)
                            last.then_inc(sem("gru_mm"), 1)
                pe.wait_ge(sem("h_new"), l * (4 * NCH) + (4 * NCH + 2))
                for t in range(NT):
                    pe.wait_ge(sem("tp_free"), l * NT + (t + 1))
                    tp(PS[:, t % CH, 0:P], HT[:, 0, t * P:(t + 1) * P], ident[:, :])
                    tp(PS[:, t % CH, P:D], HT[:, 1, t * P:(t + 1) * P], ident[:, :]).then_inc(sem("tp_done"), 1)
            ffn_pe(FFN0)
            gat_pe(GAT1)
            gat_pe(GAT2)
            ffn_pe(FFN1)


_INS = ['x', 'src', 'dst', 'edge_weight', 'L0_gnn_weight', 'L0_gnn_w_ih', 'L0_gnn_w_hh', 'L0_gnn_b_ih', 'L0_gnn_b_hh',
        'L0_ffn_Wr', 'L0_ffn_W1s', 'L0_ffn_b1s', 'L0_ffn_W2s', 'L0_ffn_b2s', 'L0_ffn_W1p', 'L0_ffn_b1p', 'L0_ffn_W2p',
        'L0_ffn_b2p', 'L1_gnn_Wl1', 'L1_gnn_Wr1', 'L1_gnn_att1', 'L1_gnn_b1', 'L1_gnn_Wl2', 'L1_gnn_Wr2', 'L1_gnn_att2',
        'L1_gnn_b2', 'L1_ffn_gamma', 'L1_ffn_beta', 'L1_ffn_Wr', 'L1_ffn_br', 'L1_ffn_W1', 'L1_ffn_b1', 'L1_ffn_W2',
        'L1_ffn_b2']


def kernel(**inputs):
    import concourse.bacc as _bacc
    from concourse.bass_utils import run_bass_kernel_spmd as _run

    nc = _bacc.Bacc("TRN2", target_bir_lowering=False, num_devices=1)
    arrays, args = {}, {}
    for name in _INS:
        array = np.ascontiguousarray(inputs[name])
        arrays[f"in_{name}_dram"] = array
        args[name] = nc.dram_tensor(f"in_{name}_dram", array.shape, mybir.dt.from_np(array.dtype), kind="ExternalInput").ap()
    out = nc.dram_tensor("out_0_dram", (NODES, D), F32, kind="ExternalOutput").ap()
    program(nc, args, out)
    r = _run(nc, [arrays], core_ids=[0])
    return r.results[0]["out_0_dram"]
```
